# Optimizing a Trainium2 kernel written in Bass

```python
import numpy as np
import jax
import jax.numpy as jnp

def _softmax(x, axis=-1):
    return jax.nn.softmax(x, axis=axis)

def _gelu(x):
    return jax.nn.gelu(x, approximate=True)

def _silu(x):
    return jax.nn.silu(x)

def _sigmoid(x):
    return jax.nn.sigmoid(x)

def _layernorm(x, axis=-1, eps=1e-05):
    m = jnp.mean(x, axis=axis, keepdims=True)
    v = jnp.var(x, axis=axis, keepdims=True)
    return (x - m) / jnp.sqrt(v + eps)

def _scatter_add(tgt, idx, src, axis=0):
    return tgt.at[idx].add(src)

def _segment_sum(src, seg, n):
    return jax.ops.segment_sum(src, seg, n)
kernel_name = 'mk_gnn_resnorm_d1_gnn_r32_fa42e3'

def setup_inputs(seed: int=0):
    np.random.seed(seed)
    _w = jnp.asarray

    def _rec_inputs():
        import jax
        import jax.numpy as jnp
        _gk = jax.random.key(seed)
        x = -0.000202 + 1 * jax.random.normal(jax.random.fold_in(_gk, 1), (3125, 64), jnp.float32)
        _s = jax.random.randint(jax.random.fold_in(_gk, 2), (50000,), 0, 3125, jnp.int32)
        _d = jax.random.randint(jax.random.fold_in(_gk, 3), (50000,), 0, 3125, jnp.int32)
        _loop = jnp.arange(3125, dtype=jnp.int32)
        src = jnp.concatenate([_s, _d, _loop])
        dst = jnp.concatenate([_d, _s, _loop])
        _o = jnp.argsort(dst, stable=True)
        src = src[_o]
        dst = dst[_o]
        edge_type_16 = jax.random.randint(jax.random.fold_in(_gk, 12), (103125,), 0, 16, jnp.int32)
        return (x, src, dst, edge_type_16)
    x, src, dst, edge_type_16 = _rec_inputs()

    def _L0_gnn_setup():
        import jax, jax.numpy as jnp
        import numpy as np
        N_NODES = 3125
        N_EDGES = 31250
        D_IN = 64
        D_OUT = 64
        N_RELS = 16
        key = jax.random.key(seed)
        k1, k2, k3, k4, k5 = jax.random.split(key, 5)
        feat = jax.random.normal(k1, (N_NODES, D_IN), dtype=jnp.float32)
        weight = jax.random.normal(k2, (N_RELS, D_IN, D_OUT), dtype=jnp.float32) * 0.05
        src = jax.random.randint(k3, (N_EDGES,), 0, N_NODES)
        dst = jax.random.randint(k4, (N_EDGES,), 0, N_NODES)
        etypes = jax.random.randint(k5, (N_EDGES,), 0, N_RELS)
        return {'feat': feat, 'weight': weight, 'src': src, 'dst': dst, 'etypes': etypes}
    _L0_gnn_all = _L0_gnn_setup()
    _L0_gnn_in = {k: v for k, v in _L0_gnn_all.items() if k in ('weight',)}
    del _L0_gnn_all
    return {'x': x, 'src': src, 'dst': dst, 'edge_type_16': edge_type_16, 'L0_gnn_weight': _L0_gnn_in['weight']}

def reference(x, src, dst, edge_type_16, L0_gnn_weight):
    import jax
    import jax.numpy as jnp

    def _L0_gnn_ref(feat, weight, src, dst, etypes):
        import jax, jax.numpy as jnp
        import numpy as np
        N_NODES = 3125
        N_EDGES = 31250
        D_IN = 64
        D_OUT = 64
        N_RELS = 16
        h = feat[src]
        n_rels = weight.shape[0]
        e, d_out = (h.shape[0], weight.shape[2])

        def step(m, rw):
            r, w_r = rw
            mask = jnp.where(etypes == r, 1.0, 0.0).astype(h.dtype)
            m = m + mask[:, None] * (h @ w_r)
            return (m, None)
        m0 = jnp.zeros((e, d_out), dtype=h.dtype)
        m, _ = jax.lax.scan(step, m0, (jnp.arange(n_rels), weight))
        out = jax.ops.segment_sum(m, dst, num_segments=feat.shape[0])
        return out
    x = _layernorm(x + _L0_gnn_ref(x, L0_gnn_weight, src, dst, edge_type_16), axis=-1)
    return x

_drawn_inputs = setup_inputs


def setup_inputs(seed=0):
    import zlib

    import numpy as np

    out = dict(_drawn_inputs(seed))
    spreads = {}
    factors = {}
    for name, (base, spread) in spreads.items():
        noise = np.random.default_rng([zlib.crc32(name.encode()), seed]).standard_normal(out[name].shape)
        drawn = base * np.exp(spread * noise) if base else spread * noise
        out[name] = jnp.asarray(drawn.astype(out[name].dtype))
    for name, factor in factors.items():
        out[name] = (out[name] * factor).astype(out[name].dtype)
    return out
```

```python
import concourse.bass as bass
from concourse import mybir
from contextlib import ExitStack


def gnn_resnorm(nc, x, src, dst, etype, weight, out):
    f32, i32, i16, bf16 = mybir.dt.float32, mybir.dt.int32, mybir.dt.int16, mybir.dt.bfloat16
    ALU, ACT, AX = mybir.AluOpType, mybir.ActivationFunctionType, mybir.AxisListType
    PE_ENG, DVE_ENG = mybir.EngineType.PE, mybir.EngineType.DVE

    N, D = x.shape
    R = weight.shape[0]
    E = src.shape[0]
    P = 128
    GT = 13
    OWN = 3
    HALF = (0, 7, GT)
    TILES = -(-E // P)
    G = TILES // GT
    assert G * GT == TILES and G % 2 == 0
    LAST = G // 2 - 1
    ROW = GT * P
    REAL = E - (G - 1) * ROW
    PAD = ROW - REAL
    WIN = P // R
    SPAN = 512 // R
    FAR = float(1 << 20)
    EPS = 1e-5
    NP = 125
    NB = N // NP
    assert NP * NB == N
    OUTW = N + SPAN
    PW = 16
    SPLIT = 3
    RP = SPLIT + 1
    XB = 4
    YB = 8
    XT = -(-NB // XB)
    YT = -(-NB // YB)
    RQ = R // 2

    x_parts = nc.dram_tensor("x_parts", [N, RP * D], bf16, kind="Internal").ap()

    ctx = ExitStack()
    with ctx:
        def sb(name, shape, dt=f32):
            return ctx.enter_context(nc.sbuf_tensor(name, shape, dt))

        def sem(name):
            return ctx.enter_context(nc.semaphore(name))

        def sem2(name):
            return [sem(f"{name}{u}") for u in range(2)]

        src_i = sb("src_i", [G, ROW], i32)
        dst_i = sb("dst_i", [G, ROW], i32)
        et_i = sb("et_i", [G, ROW], i32)
        far_i = sb("far_i", [1, PAD], i32)
        src_f = sb("src_f", [G, ROW])
        dst_f = sb("dst_f", [G, ROW])
        et_f = sb("et_f", [G, ROW])
        krel_f = sb("krel_f", [G, ROW])
        key_f = krel_f
        tmin = sb("tmin", [G, GT])
        tmax = sb("tmax", [G, GT])
        base = sb("base", [G, 2])
        start = sb("start", [G, GT])
        wstart = sb("wstart", [G, GT])
        reach = sb("reach", [G, GT])
        far = sb("far", [G, GT])
        shift = sb("shift", [G, GT])
        par = sb("par", [G, PW], i32)
        par_row = sb("par_row", [1, G * PW], i32)
        any_far = sb("any_far", [1, 1], i32)
        idx = sb("idx", [P, TILES], i32)
        krel = sb("krel", [P, TILES])
        gidx = sb("gidx", [P, 2, GT], i32)
        ident = sb("ident", [P, P])
        ramp = sb("ramp", [P, P], bf16)
        node = sb("node", [NP, NB])
        zeros = sb("zeros", [P, 512], bf16)
        w_pair = sb("w_pair", [2 * D, RQ, D])
        x_sb = sb("x_sb", [NP, NB, D])
        x_rest = sb("x_rest", [NP, NB, D])
        xp = sb("xp", [NP, NB, RP, D], bf16)
        outT = sb("outT", [D, OUTW])
        rows = sb("rows", [P, 2, GT, RP * D], bf16)
        onehot = sb("onehot", [P, 2, GT, P], bf16)
        src_b = sb("src_b", [NP, 2, OWN * P], i32)
        src_h = sb("src_h", [NP, 2, OWN * P], i16)
        pick = sb("pick", [NP, 2, NB, OWN * P], bf16)
        aggT = sb("aggT", [2 * D, 2, 2 * SPAN, RQ])
        y, sq = x_sb, x_rest
        mean = sb("mean", [NP, NB])
        var = sb("var", [NP, NB])
        rstd = sb("rstd", [NP, NB])
        g_dst_f = krel_f
        g_dst = sb("g_dst", [P, TILES])
        g_et = sb("g_et", [P, TILES])
        g_idx = sb("g_idx", [P, 1], i32)
        g_rows = sb("g_rows", [P, D])
        g_rowsT = sb("g_rowsT", [D, P])
        g_w = sb("g_w", [D, R, D])
        g_rel = sb("g_rel", [P, R])
        g_all = sb("g_all", [P, R, D])
        g_msg = sb("g_msg", [P, D])
        g_ramp = sb("g_ramp", [P, NB, NP])
        g_hot = sb("g_hot", [P, NB, NP])

        agg = [ctx.enter_context(nc.psum_tensor(f"agg{u}", [P, 2, 512], f32)) for u in range(2)]
        rel = ctx.enter_context(nc.psum_tensor("rel", [P, 512], f32))
        own = [ctx.enter_context(nc.psum_tensor(f"own{h}", [P, 512], f32)) for h in range(3)]

        src_in, dst_in, et_in = sem("src_in"), sem("dst_in"), sem("et_in")
        far_set, w_in, x_in = sem("far_set"), sem("w_in"), sem("x_in")
        ident_zero, const_set, zeros_set = sem("ident_zero"), sem("const_set"), sem("zeros_set")
        src_cast, srcT_done, idx_done = sem("src_cast"), sem("srcT_done"), sem("idx_done")
        split, parts_out = sem("split"), sem("parts_out")
        prep = sem("prep")
        krel_cast, krelT_done, krel_done = sem("krel_cast"), sem("krelT_done"), sem("krel_done")
        par_set, par_in, any_set = sem("par_set"), sem("par_in"), sem("any_set")
        xT_done, xT_taken = sem("xT_done"), sem("xT_taken")
        gidx_ready, rows_in = sem2("gidx_ready"), sem2("rows_in")
        src_b_in, src_h_ready, pick_ready = sem2("src_b_in"), sem2("src_h_ready"), sem2("pick_ready")
        own_done, own_rows = sem2("own_done"), sem2("own_rows")
        onehot_ready, agg_ready, agg_copied = sem2("onehot_ready"), sem2("agg_ready"), sem2("agg_copied")
        rel_ready, rel_added = sem2("rel_ready"), sem("rel_added")
        yT_done, y_taken, norm = sem("yT_done"), sem("y_taken"), sem("norm")
        y_ready, out_done = sem("y_ready"), sem("out_done")
        g_prep, g_setT, g_set, g_w_in = sem("g_prep"), sem("g_setT"), sem("g_set"), sem("g_w_in")
        g_idx_ready, g_rows_in = sem("g_idx_ready"), sem("g_rows_in")
        g_T_done, g_T_taken, g_all_done, g_msg_ready = sem("g_T_done"), sem("g_T_taken"), sem("g_all_done"), sem("g_msg_ready")
        g_step, g_added, g_sum = sem("g_step"), sem("g_added"), sem("g_sum")
        block = ctx.enter_context(nc.Block())

        def tile_view(t):
            return t[:, :].rearrange("g (j e) -> g j e", e=P)

        def group_loop(eng, body, first=0, last=LAST + 1):
            if first == 0:
                body(0)
                first = 1
            with eng.Fori(first, last) as i:
                body(i)

        def is_first(i):
            return isinstance(i, int) and i == 0

        def go_general(eng):
            eng.wait_ge(any_set, 1)
            v = nc.values_load_multi_w_load_instructions(any_far[0:1, 0:1], engines=[eng.engine], min_val=0, max_val=int(FAR),
                                                         skip_runtime_bounds_check_because="zero or FAR")[1][0]
            return eng.If(v > 0)

        @block.sync
        def _(sp):
            def load(tile, a, s, pad_src):
                sp.dma_start(tile[0:G - 1, :], a[0:(G - 1) * ROW].rearrange("(g e) -> g e", e=ROW)).then_inc(s, 16)
                sp.dma_start(tile[G - 1:G, 0:REAL], a[(G - 1) * ROW:E].rearrange("(o e) -> o e", o=1)).then_inc(s, 16)
                sp.dma_start(tile[G - 1:G, REAL:ROW], pad_src).then_inc(s, 16)

            def row(a):
                return a[E - PAD:E].rearrange("(o e) -> o e", o=1)

            load(src_i, src, src_in, row(src))
            load(dst_i, dst, dst_in, row(dst))
            sp.wait_ge(far_set, 1)
            load(et_i, etype, et_in, far_i[:, :])
            sp.wait_ge(split, 5)
            sp.dma_start(x_parts.rearrange("(p b) d -> p (b d)", b=NB),
                         xp[:, :, :, :].rearrange("p b s d -> p (b s d)")).then_inc(parts_out, 16)

            def spread_sources(i, u):
                if not is_first(i):
                    sp.wait_ge(src_h_ready[u], i)
                a = src[bass.ds(i * (2 * ROW) + u * ROW, OWN * P)]
                sp.dma_start(src_b[:, u, :], a.rearrange("(o e) -> o e", o=1).to_broadcast([NP, OWN * P])).then_inc(src_b_in[u], 16)

            def turn(i):
                spread_sources(i, 0)
                spread_sources(i, 1)
            turn(0)
            sp.wait_ge(par_set, 3)
            sp.dma_start(par_row[:, :], par[:, :]).then_inc(par_in, 16)
            group_loop(sp, turn, first=1)
            with go_general(sp):
                sp.dma_start(g_w[:, :, :], weight.rearrange("r k d -> k r d")).then_inc(g_w_in, 16)
            sp.wait_ge(y_ready, 1)
            sp.dma_start(out.rearrange("(p b) d -> p b d", b=NB), y[:, :, :]).then_inc(out_done, 16)
            sp.wait_ge(out_done, 16)

        @block.gpsimd
        def _(pool):
            pool.memset(far_i[:, :], -int(FAR)).then_inc(far_set, 1)
            pool.memset(ident[:, :], 0.0).then_inc(ident_zero, 1)
            pool.iota(ramp[:, :], pattern=[[1, P]], base=0, channel_multiplier=0,
                      allow_small_or_imprecise_dtypes=True).then_inc(const_set, 1)
            pool.wait_ge(ident_zero, 1)
            pool.affine_select(out=ident[:, :], in_=ident[:, :], compare_op=ALU.not_equal, fill=1.0,
                               base=0, pattern=[[-1, P]], channel_multiplier=1).then_inc(const_set, 1)
            pool.iota(node[:, :], pattern=[[1, NB]], base=0, channel_multiplier=NB,
                      allow_small_or_imprecise_dtypes=True).then_inc(const_set, 1)
            pool.memset(zeros[:, :], 0.0).then_inc(zeros_set, 1)
            pool.wait_ge(parts_out, 16)

            def fetch(i, u):
                if not is_first(i):
                    pool.wait_ge(agg_ready[u], i)
                pool.wait_ge(gidx_ready[u], i + 1)
                pool.nop(nofuse=True)
                for j in range(OWN, GT):
                    pool.indirect_dma_start(
                        rows[:, u, j, :], None, x_parts,
                        bass.IndirectOffsetOnAxis(ap=gidx[:, u, j:j + 1], axis=0)).then_inc(rows_in[u], 16)

            def turn(i):
                fetch(i, 0)
                fetch(i, 1)
            group_loop(pool, turn)

            with go_general(pool):
                pool.iota(g_ramp[:, :, :], pattern=[[1, NB], [NB, NP]], base=0, channel_multiplier=0,
                          allow_small_or_imprecise_dtypes=True).then_inc(g_set, 1)
                with pool.Fori(0, TILES) as t:
                    pool.wait_ge(g_idx_ready, t + 1)
                    pool.nop(nofuse=True)
                    pool.indirect_dma_start(g_rows[:, :], None, x,
                                            bass.IndirectOffsetOnAxis(ap=g_idx[:, 0:1], axis=0)).then_inc(g_rows_in, 16)

        @block.scalar
        def _(act):
            act.dma_start(x_sb[:, :, :], x.rearrange("(p b) d -> p b d", b=NB)).then_inc(x_in, 16)
            for q in range(2):
                act.dma_start(w_pair[q * D:(q + 1) * D, :, :],
                              weight.rearrange("(q two) k d -> two k q d", two=2)[q]).then_inc(w_in, 16)
            act.wait_ge(src_in, 48)
            act.activation(src_f[:, :], src_i[:, :], ACT.Copy).then_inc(src_cast, 1)
            act.wait_ge(srcT_done, 1)
            iv = idx[:, :].rearrange("p (g j) -> p j g", j=GT)
            for n, (j0, j1) in enumerate(((0, 8), (8, GT))):
                act.activation(iv[:, j0:j1, :], own[n][:, 0:(j1 - j0) * G].rearrange("p (j g) -> p j g", g=G), ACT.Copy).then_inc(idx_done, 1)
            act.wait_ge(idx_done, 2)

            def group_indices(i, u):
                if not is_first(i):
                    act.wait_ge(rows_in[u], i * (16 * (GT - OWN)))
                act.activation(gidx[:, u, :], idx[:, bass.ds(i * (2 * GT) + u * GT, GT)], ACT.Copy).then_inc(gidx_ready[u], 1)

            def narrow_sources(i, u):
                act.wait_ge(src_b_in[u], (i + 1) * 16)
                if not is_first(i):
                    act.wait_ge(pick_ready[u], i)
                act.activation(src_h[:, u, :], src_b[:, u, :], ACT.Copy).then_inc(src_h_ready[u], 1)

            def take_agg(i, u):
                act.wait_ge(agg_ready[u], i + 1)
                if not is_first(i):
                    act.wait_ge(rel_ready[u], i)
                for q in range(2):
                    act.activation(aggT[q * D:(q + 1) * D, u, :, :],
                                   agg[u][q * D:(q + 1) * D, :, :].rearrange("d h (n r two) -> d (h n) r two", r=RQ, two=2)[:, :, :, q],
                                   ACT.Copy).then_inc(agg_copied[u], 1)

            def take_own(i, u):
                for h in range(OWN):
                    act.wait_ge(own_done[u], i * OWN + (h + 1))
                    act.activation(rows[:, u, h, 0:SPLIT * D], own[h][:, 0:SPLIT * D], ACT.Copy).then_inc(own_rows[u], 1)
                    act.activation(rows[:, u, h, SPLIT * D:RP * D], own[h][:, 0:D], ACT.Copy).then_inc(own_rows[u], 1)

            group_indices(0, 0)
            group_indices(0, 1)
            narrow_sources(0, 0)
            narrow_sources(0, 1)
            take_own(0, 0)

            def turn(i, more=True):
                if more:
                    narrow_sources(i + 1, 0)
                    group_indices(i + 1, 0)
                take_agg(i, 0)
                take_own(i, 1)
                if more:
                    narrow_sources(i + 1, 1)
                    group_indices(i + 1, 1)
                take_agg(i, 1)
                if more:
                    take_own(i + 1, 0)
            group_loop(act, turn, last=LAST)
            turn(LAST, more=False)

            with go_general(act):
                with act.Fori(0, TILES) as t:
                    act.wait_ge(g_step, t + 1)
                    act.activation(g_idx[:, :], idx[:, bass.ds(t, 1)], ACT.Copy).then_inc(g_idx_ready, 1)
                    act.wait_ge(g_T_done, t + 1)
                    act.activation(g_rowsT[:, :], rel[0:D, 0:P], ACT.Copy).then_inc(g_T_taken, 1)
            act.wait_ge(norm, 5)
            act.activation(rstd[:, :], var[:, :], ACT.Sqrt).then_inc(norm, 1)

        @block.vector
        def _(dve):
            v = nc.vector
            dve.wait_ge(x_in, 16)
            v.tensor_copy(xp[:, :, 0, :], x_sb[:, :, :]).then_inc(split, 1)
            dve.wait_ge(split, 1)
            v.tensor_tensor(x_rest[:, :, :], x_sb[:, :, :], xp[:, :, 0, :], ALU.subtract).then_inc(split, 1)
            dve.wait_ge(split, 2)
            v.tensor_copy(xp[:, :, 1, :], x_rest[:, :, :]).then_inc(split, 1)
            v.tensor_copy(xp[:, :, RP - 1, :], x_sb[:, :, :]).then_inc(split, 1)
            dve.wait_ge(split, 4)
            v.tensor_tensor(xp[:, :, 2, :], x_rest[:, :, :], xp[:, :, 1, :], ALU.subtract).then_inc(split, 1)

            def picks(i, u):
                dve.wait_ge(src_h_ready[u], i + 1)
                if not is_first(i):
                    dve.wait_ge(own_done[u], i * OWN)
                for b in range(NB):
                    last = v.tensor_scalar(pick[:, u, b, :], src_h[:, u, :], node[:, b:b + 1], None, ALU.is_equal)
                last.then_inc(pick_ready[u], 1)

            steps = [0]

            def step(ins):
                steps[0] += 1
                ins.then_inc(prep, 1)

            def settle():
                dve.wait_ge(prep, steps[0])

            dve.wait_ge(dst_in, 48)
            step(v.tensor_copy(dst_f[:, :], dst_i[:, :]))
            settle()
            step(v.tensor_reduce(tmin[:, :], tile_view(dst_f), AX.X, ALU.min))
            step(v.tensor_reduce(tmax[:, :], tile_view(dst_f), AX.X, ALU.max))
            settle()
            for h in range(2):
                step(v.tensor_reduce(base[:, h:h + 1], tmin[:, HALF[h]:HALF[h + 1]], AX.X, ALU.min))
            settle()
            for h in range(2):
                a, b = HALF[h], HALF[h + 1]
                step(v.tensor_scalar(start[:, a:b], tmin[:, a:b], base[:, h:h + 1], float(SPAN - WIN), ALU.subtract, ALU.min))
            settle()
            v.tensor_scalar(par[:, 0:GT], start[:, :], float(R), None, ALU.mult).then_inc(par_set, 1)
            v.tensor_copy(par[:, GT:GT + 2], base[:, :]).then_inc(par_set, 1)
            for h in range(2):
                a, b = HALF[h], HALF[h + 1]
                step(v.tensor_scalar(wstart[:, a:b], start[:, a:b], base[:, h:h + 1], None, ALU.add))
            settle()
            step(v.tensor_tensor(reach[:, :], tmax[:, :], wstart[:, :], ALU.subtract))
            settle()
            step(v.tensor_scalar(far[:, :], reach[:, :], float(WIN), FAR, ALU.is_ge, ALU.mult))
            settle()
            v.tensor_reduce(par[:, GT + 2:PW], far[:, :], AX.X, ALU.max).then_inc(par_set, 1)
            step(v.scalar_tensor_tensor(shift[:, :], wstart[:, :], float(R), far[:, :], ALU.mult, ALU.add))
            dve.wait_ge(et_in, 48)
            step(v.tensor_copy(et_f[:, :], et_i[:, :]))
            settle()
            step(v.scalar_tensor_tensor(key_f[:, :], dst_f[:, :], float(R), et_f[:, :], ALU.mult, ALU.add))
            settle()
            v.tensor_tensor(tile_view(krel_f), tile_view(key_f),
                            shift[:, :].rearrange("g (j o) -> g j o", o=1).to_broadcast([G, GT, P]), ALU.subtract).then_inc(krel_cast, 1)
            dve.wait_ge(const_set, 3)
            picks(0, 0)
            dve.wait_ge(krelT_done, 1)
            kv = krel[:, :].rearrange("p (g j) -> p j g", j=GT)
            for n, (j0, j1) in enumerate(((0, 8), (8, GT))):
                v.tensor_copy(kv[:, j0:j1, :], own[n + 1][:, 0:(j1 - j0) * G].rearrange("p (j g) -> p j g", g=G)).then_inc(krel_done, 1)
            v.memset(outT[:, N:OUTW], 0.0).then_inc(xT_taken, 1)
            ov = outT[:, 0:N].rearrange("d (p b) -> d b p", b=NB)
            for n in range(XT):
                b0, k = n * XB, min(XB, NB - n * XB)
                dve.wait_ge(xT_done, n + 1)
                v.tensor_copy(ov[:, b0:b0 + k, :], agg[n % 2][0:D, n // 2 % 2, 0:k * NP].rearrange("d (b p) -> d b p", p=NP)).then_inc(xT_taken, 1)
            dve.wait_ge(krel_done, 2)

            def onehots(i, u):
                if not is_first(i):
                    dve.wait_ge(agg_ready[u], i)
                for j in range(GT):
                    last = v.tensor_scalar(onehot[:, u, j, :], ramp[:, :],
                                           krel[:, bass.ds(i * (2 * GT) + (u * GT + j), 1)], None, ALU.is_equal)
                last.then_inc(onehot_ready[u], 1)

            def half_starts(i, u):
                return nc.values_load_multi_w_load_instructions(
                    par_row[0:1, bass.ds(i * (2 * PW) + (u * PW + GT), 2)], engines=[DVE_ENG], min_val=0, max_val=N - 1,
                    skip_runtime_bounds_check_because="a node index of the edge list")[1]

            def add_rel(i, u, at):
                dve.wait_ge(rel_ready[u], i + 1)
                for h in range(2):
                    if not (is_first(i) and u == 0 and h == 0):
                        dve.wait_ge(rel_added, i * 4 + (2 * u + h))
                    o = outT[:, bass.ds(at[h], SPAN)]
                    v.tensor_tensor(o, o, rel[0:D, h * SPAN:(h + 1) * SPAN], ALU.add).then_inc(rel_added, 1)

            onehots(0, 0)
            picks(0, 1)
            dve.wait_ge(xT_taken, 1 + XT)
            dve.wait_ge(par_in, 16)
            v.tensor_reduce(any_far[:, :], par_row[:, :].rearrange("o (g w) -> o g w", w=PW)[:, :, PW - 1:PW].rearrange("o g w -> o (g w)"),
                            AX.X, ALU.max).then_inc(any_set, 1)

            def turn(i, more=True):
                at = [half_starts(i, u) for u in range(2)]
                onehots(i, 1)
                if more:
                    picks(i + 1, 0)
                add_rel(i, 0, at[0])
                if more:
                    onehots(i + 1, 0)
                    picks(i + 1, 1)
                add_rel(i, 1, at[1])
            group_loop(dve, turn, last=LAST)
            turn(LAST, more=False)

            for n in range(YT):
                b0, k = n * YB, min(YB, NB - n * YB)
                dve.wait_ge(yT_done, n + 1)
                v.tensor_copy(y[:, b0:b0 + k, :], own[n % 2][0:NP, 0:k * D].rearrange("p (b d) -> p b d", d=D)).then_inc(y_taken, 1)
            dve.wait_ge(y_taken, YT)

            with go_general(dve):
                v.tensor_scalar(shift[:, :], far[:, :], -FAR, None, ALU.add).then_inc(g_prep, 1)
                dve.wait_ge(g_prep, 1)
                v.tensor_tensor(tile_view(g_dst_f), tile_view(dst_f),
                                shift[:, :].rearrange("g (j o) -> g j o", o=1).to_broadcast([G, GT, P]), ALU.add).then_inc(g_prep, 1)
                for n, a in enumerate((g_dst, g_et)):
                    av = a[:, :].rearrange("p (g j) -> p j g", j=GT)
                    dve.wait_ge(g_setT, n + 1)
                    for m, (j0, j1) in enumerate(((0, 8), (8, GT))):
                        v.tensor_copy(av[:, j0:j1, :], own[m][:, 0:(j1 - j0) * G].rearrange("p (j g) -> p j g", g=G)).then_inc(g_set, 1)
                dve.wait_ge(g_set, 5)
                v.memset(g_msg[:, :], 0.0).then_inc(g_step, 1)
                with dve.Fori(0, TILES) as t:
                    dve.wait_ge(g_step, t + 1)
                    v.tensor_scalar(g_rel[:, :], ramp[:, 0:R], g_et[:, bass.ds(t, 1)], None, ALU.is_equal).then_inc(g_msg_ready, 1)
                    v.tensor_scalar(g_hot[:, :, :], g_ramp[:, :, :], g_dst[:, bass.ds(t, 1)], None, ALU.is_equal).then_inc(g_msg_ready, 1)
                    dve.wait_ge(g_msg_ready, t * 5 + 1)
                    dve.wait_ge(g_all_done, t + 1)
                    for m in range(2):
                        r0 = m * (R // 2)
                        v.tensor_tensor(g_all[:, r0:r0 + R // 2, :], own[m][:, :].rearrange("p (r d) -> p r d", d=D),
                                        g_rel[:, r0:r0 + R // 2].rearrange("p (r o) -> p r o", o=1).to_broadcast([P, R // 2, D]),
                                        ALU.mult).then_inc(g_msg_ready, 1)
                    dve.wait_ge(g_msg_ready, t * 5 + 4)
                    v.tensor_reduce(g_msg[:, :], g_all[:, :, :].rearrange("p r d -> p d r"), AX.X, ALU.add).then_inc(g_msg_ready, 1)
                dve.wait_ge(g_added, 1)
                yv = y[:, :, :].rearrange("p b d -> p (b d)")
                for n in range(YT):
                    c0, c1 = n * YB * D, min((n + 1) * YB, NB) * D
                    v.tensor_tensor(yv[:, c0:c1], yv[:, c0:c1], agg[n // 2][0:NP, n % 2, 0:c1 - c0], ALU.add).then_inc(g_sum, 1)
                dve.wait_ge(g_sum, YT)

            v.tensor_reduce(mean[:, :], y[:, :, :], AX.X, ALU.add).then_inc(norm, 1)
            dve.wait_ge(norm, 1)
            v.scalar_tensor_tensor(y[:, :, :], mean[:, :].rearrange("p (b o) -> p b o", o=1).to_broadcast([NP, NB, D]), -1.0 / D,
                                   y[:, :, :], ALU.mult, ALU.add).then_inc(norm, 1)
            dve.wait_ge(norm, 2)
            v.tensor_tensor(sq[:, :, :], y[:, :, :], y[:, :, :], ALU.mult).then_inc(norm, 1)
            dve.wait_ge(norm, 3)
            v.tensor_reduce(mean[:, :], sq[:, :, :], AX.X, ALU.add).then_inc(norm, 1)
            dve.wait_ge(norm, 4)
            v.tensor_scalar(var[:, :], mean[:, :], 1.0 / D, EPS, ALU.mult, ALU.add).then_inc(norm, 1)
            dve.wait_ge(norm, 6)
            v.reciprocal(rstd[:, :], rstd[:, :]).then_inc(norm, 1)
            dve.wait_ge(norm, 7)
            v.tensor_tensor(y[:, :, :], y[:, :, :], rstd[:, :].rearrange("p (b o) -> p b o", o=1).to_broadcast([NP, NB, D]),
                            ALU.mult).then_inc(y_ready, 1)

        @block.tensor
        def _(pe):
            def edge_transposes(a, banks, done):
                for j in range(GT):
                    last = nc.tensor.transpose(banks[j // 8][:, (j % 8) * G:(j % 8 + 1) * G],
                                               a[:, j * P:(j + 1) * P], ident[0:G, 0:G])
                last.then_inc(done, 1)

            pe.wait_ge(const_set, 3)
            pe.wait_ge(src_cast, 1)
            edge_transposes(src_f, own[0:2], srcT_done)
            pe.wait_ge(x_in, 16)
            for n in range(XT):
                if n >= 4:
                    pe.wait_ge(xT_taken, n - 2)
                for b in range(n * XB, min((n + 1) * XB, NB)):
                    c = (b - n * XB) * NP
                    last = nc.tensor.transpose(agg[n % 2][0:D, n // 2 % 2, c:c + NP], x_sb[:, b, :], ident[0:NP, 0:NP])
                last.then_inc(xT_done, 1)
                if n == 3:
                    pe.wait_ge(idx_done, 2)
                    pe.wait_ge(krel_cast, 1)
                    edge_transposes(krel_f, own[1:3], krelT_done)

            def fetch_own(i, u):
                pe.wait_ge(pick_ready[u], i + 1)
                if u == 1:
                    pe.wait_ge(own_rows[0], (i + 1) * (2 * OWN))
                elif not is_first(i):
                    pe.wait_ge(own_rows[1], i * (2 * OWN))
                for h in range(OWN):
                    for b in range(NB):
                        last = nc.tensor.matmul(own[h][:, 0:SPLIT * D], pick[:, u, b, h * P:(h + 1) * P],
                                                xp[:, b, 0:SPLIT, :].rearrange("p s d -> p (s d)"), start=(b == 0), stop=(b == NB - 1))
                    last.then_inc(own_done[u], 1)

            def window_starts(i, u):
                return nc.values_load_multi_w_load_instructions(
                    par_row[0:1, bass.ds(i * (2 * PW) + u * PW, GT)], engines=[PE_ENG], min_val=0, max_val=(SPAN - WIN) * R,
                    skip_runtime_bounds_check_because="clamped when it was worked out")[1]

            def aggregate(i, u, at):
                if not is_first(i):
                    pe.wait_ge(agg_copied[u], i * 2)
                for h in range(2):
                    nc.tensor.matmul(agg[u][:, h, :], zeros[:, 0:P], zeros[:, :], start=True, stop=False, skip_group_check=True)
                pe.wait_ge(onehot_ready[u], i + 1)
                pe.wait_ge(own_rows[u], (i + 1) * (2 * OWN))
                for j in range(GT):
                    if j == OWN:
                        pe.wait_ge(rows_in[u], (i + 1) * (16 * (GT - OWN)))
                    for s in range(SPLIT):
                        last = nc.tensor.matmul(
                            agg[u][:, int(j >= HALF[1]), bass.ds(at[j], P)],
                            rows[:, u, j, s * D:(s + 2) * D], onehot[:, u, j, :],
                            start=False, stop=(j + 1 in HALF and s == SPLIT - 1), skip_group_check=True)
                last.then_inc(agg_ready[u], 1)

            def relate(i, u):
                pe.wait_ge(agg_copied[u], (i + 1) * 2)
                if not (is_first(i) and u == 0):
                    pe.wait_ge(rel_added, i * 4 + 2 * u)
                for q in range(RQ):
                    last = nc.tensor.matmul(rel[0:D, 0:2 * SPAN], w_pair[:, q, :], aggT[:, u, :, q],
                                            start=(q == 0), stop=(q == RQ - 1))
                last.then_inc(rel_ready[u], 1)

            pe.wait_ge(krel_done, 2)
            fetch_own(0, 0)
            pe.wait_ge(w_in, 32)
            pe.wait_ge(zeros_set, 1)
            pe.wait_ge(xT_taken, 1 + XT)
            pe.wait_ge(par_in, 16)

            aggregate(0, 0, window_starts(0, 0))

            def turn(i, more=True):
                at = window_starts(i, 1)
                fetch_own(i, 1)
                relate(i, 0)
                aggregate(i, 1, at)
                if more:
                    at = window_starts(i + 1, 0)
                    fetch_own(i + 1, 0)
                relate(i, 1)
                if more:
                    aggregate(i + 1, 0, at)
            group_loop(pe, turn, last=LAST)
            turn(LAST, more=False)

            pe.wait_ge(rel_added, 2 * G)
            yv = outT[:, 0:N].rearrange("d (p b) -> d b p", b=NB)
            for n in range(YT):
                if n >= 2:
                    pe.wait_ge(y_taken, n - 1)
                for b in range(n * YB, min((n + 1) * YB, NB)):
                    c = (b - n * YB) * D
                    last = nc.tensor.transpose(own[n % 2][0:NP, c:c + D], yv[:, b, :], ident[0:D, 0:D])
                last.then_inc(yT_done, 1)

            with go_general(pe):
                pe.wait_ge(g_prep, 2)
                pe.wait_ge(y_taken, YT)
                edge_transposes(g_dst_f, own[0:2], g_setT)
                pe.wait_ge(g_set, 3)
                edge_transposes(et_f, own[0:2], g_setT)
                for n in range(4):
                    nc.tensor.matmul(agg[n // 2][:, n % 2, :], zeros[:, 0:P], zeros[:, :], start=True, stop=False, skip_group_check=True)
                pe.wait_ge(g_set, 5)
                pe.wait_ge(g_w_in, 16)
                with pe.Fori(0, TILES) as t:
                    pe.wait_ge(g_rows_in, (t + 1) * 16)
                    pe.nop(nofuse=True)
                    nc.tensor.transpose(rel[0:D, 0:P], g_rows[:, :], ident[:, :]).then_inc(g_T_done, 1)
                    pe.wait_ge(g_T_taken, t + 1)
                    pe.nop(nofuse=True)
                    for m in range(2):
                        last = nc.tensor.matmul(own[m][:, :], g_rowsT[:, :], g_w[:, m * (R // 2):(m + 1) * (R // 2), :], start=True, stop=True)
                    last.then_inc(g_all_done, 1)
                    pe.wait_ge(g_msg_ready, (t + 1) * 5)
                    for b in range(NB):
                        n, c = b // YB, (b % YB) * D
                        last = nc.tensor.matmul(agg[n // 2][0:NP, n % 2, c:c + D], g_hot[:, b, :], g_msg[:, :],
                                                start=False, stop=False, skip_group_check=True)
                    last.then_inc(g_step, 1)
                nc.tensor.matmul(rel[0:D, 0:D], zeros[:, 0:D], zeros[:, 0:D], start=True, stop=True).then_inc(g_added, 1)


def kernel(x, src, dst, edge_type_16, L0_gnn_weight):
    import numpy as np
    import concourse.bacc as bacc
    from concourse import mybir as mb
    from concourse.bass_utils import run_bass_kernel_spmd

    nc = bacc.Bacc("TRN2", target_bir_lowering=False, num_devices=1)
    arrays = {"x": x, "src": src, "dst": dst, "edge_type": edge_type_16, "weight": L0_gnn_weight}
    arrays = {f"in_{k}": np.ascontiguousarray(v) for k, v in arrays.items()}
    args = [nc.dram_tensor(k, v.shape, mb.dt.from_np(v.dtype), kind="ExternalInput").ap() for k, v in arrays.items()]
    out = nc.dram_tensor("out", arrays["in_x"].shape, mb.dt.float32, kind="ExternalOutput").ap()
    gnn_resnorm(nc, *args, out)
    return run_bass_kernel_spmd(nc, [arrays], core_ids=[0]).results[0]["out"]
```

```python
import concourse.bass as bass
from concourse import mybir
from contextlib import ExitStack


def gnn_resnorm(nc, x, src, dst, etype, weight, out):
    f32, i32, f16, bf16 = mybir.dt.float32, mybir.dt.int32, mybir.dt.float16, mybir.dt.bfloat16
    ALU, ACT, AX = mybir.AluOpType, mybir.ActivationFunctionType, mybir.AxisListType
    PE_ENG, DVE_ENG = mybir.EngineType.PE, mybir.EngineType.DVE

    N, D = x.shape
    R = weight.shape[0]
    E = src.shape[0]
    P = 128
    GT = 13
    OWN = (3, 3)
    LATE = GT - 3
    assert max(OWN) <= 3
    HALF = (0, 7, GT)
    TILES = -(-E // P)
    G = TILES // GT
    assert G * GT == TILES and G % 2 == 0
    LAST = G // 2 - 1
    ROW = GT * P
    REAL = E - (G - 1) * ROW
    PAD = ROW - REAL
    WIN = 7
    KEYS = WIN * R
    SPAN = 512 // R
    FAR = float(1 << 20)
    EPS = 1e-5
    NP = 125
    NB = N // NP
    assert NP * NB == N
    MID = N // 2
    OUTW = N + SPAN
    PW = 16
    SPLIT = 3
    RP = SPLIT + 1
    CUT = 3
    CUTW = [-(-n * P // (2 * CUT)) * 2 for n in OWN]
    OWNW = [CUT * w for w in CUTW]
    GAP = 2
    APICK = 5
    VPICK = NB - APICK
    XHALF = (0, 13, NB)
    XB = 4
    XT = -(-NB // XB)
    YCUT = (0, 8, 16, 21, NB)
    YT = len(YCUT) - 1
    YB = 8
    RQ = R // 2

    x_parts = nc.dram_tensor("x_parts", [N, RP * D], bf16, kind="Internal").ap()

    ctx = ExitStack()
    with ctx:
        def sb(name, shape, dt=f32):
            return ctx.enter_context(nc.sbuf_tensor(name, shape, dt))

        def sem(name):
            return ctx.enter_context(nc.semaphore(name))

        def sem2(name):
            return [sem(f"{name}{u}") for u in range(2)]

        src_i = sb("src_i", [G, ROW], i32)
        dst_i = sb("dst_i", [G, ROW], i32)
        et_i = sb("et_i", [G, ROW], i32)
        far_i = sb("far_i", [1, PAD], i32)
        src_f = sb("src_f", [G, ROW])
        dst_f = sb("dst_f", [G, ROW])
        et_f = sb("et_f", [G, ROW])
        krel_f = src_f
        key_f = krel_f
        tmin = sb("tmin", [G, GT])
        tmax = sb("tmax", [G, GT])
        base = sb("base", [G, 2])
        start = sb("start", [G, GT])
        wstart = sb("wstart", [G, GT])
        reach = sb("reach", [G, GT])
        far = sb("far", [G, GT])
        shift = sb("shift", [G, GT])
        par = sb("par", [G, PW], i32)
        par_row = sb("par_row", [1, G * PW], i32)
        any_far = sb("any_far", [1, 1], i32)
        idx = sb("idx", [P, TILES], i32)
        krel = sb("krel", [P, TILES])
        gidx = sb("gidx", [P, 2, GT], i32)
        ident = sb("ident", [P, P])
        ramp = sb("ramp", [P, WIN, R + GAP], bf16)
        node = sb("node", [NP, NB])
        zeros = sb("zeros", [P, 1024], bf16)
        w_pair = sb("w_pair", [2 * D, RQ, D])
        x_sb = sb("x_sb", [NP, NB, D])
        x_rest = sb("x_rest", [NP, NB, D])
        xp = sb("xp", [NP, NB, RP, D], bf16)
        outT = sb("outT", [D, OUTW])
        rows = sb("rows", [P, 2, GT, RP * D], bf16)
        onehot = sb("onehot", [P, 2, GT, KEYS], bf16)
        src_b = [sb(f"src_b{u}", [NP, OWNW[u]], i32) for u in range(2)]
        src_h = [sb(f"src_h{u}", [NP, CUT, CUTW[u] + GAP], f16) for u in range(2)]
        pick_all = [sb(f"pick{u}", [P, NB * OWNW[u]], bf16) for u in range(2)]
        pick = [pick_all[u][0:NP, :].rearrange("p (b e) -> p b e", b=NB) for u in range(2)]
        away = sb("away", [NP, APICK, max(OWNW)], bf16)
        node_neg = sb("node_neg", [NP, NB])
        one = sb("one", [NP, 1])
        aggT = sb("aggT", [2 * D, 2, 2 * SPAN, RQ])
        y, sq = x_sb, x_rest
        w_mean = sb("w_mean", [2 * D, RQ])
        x_mean = sb("x_mean", [NP, NB])
        sqsum = sb("sqsum", [NP, NB])
        var = sb("var", [NP, NB])
        std = sb("std", [NP, NB])
        rstd = sb("rstd", [NP, NB])
        g_dst_f = krel_f
        g_dst = sb("g_dst", [P, TILES])
        g_et = sb("g_et", [P, TILES])
        g_idx = sb("g_idx", [P, 1], i32)
        g_rows = sb("g_rows", [P, D])
        g_rowsT = sb("g_rowsT", [D, P])
        g_w = sb("g_w", [D, R, D])
        g_rel = sb("g_rel", [P, R])
        g_all = sb("g_all", [P, R, D])
        g_msg = sb("g_msg", [P, D])
        g_ramp = sb("g_ramp", [P, NB, NP])
        g_hot = pick_all[1][:, 0:2 * N].bitcast(f32).rearrange("p (b n) -> p b n", b=NB)

        agg = [ctx.enter_context(nc.psum_tensor(f"agg{u}", [P, 2, 512], f32)) for u in range(2)]
        rel = ctx.enter_context(nc.psum_tensor("rel", [P, 512], f32))
        own = [ctx.enter_context(nc.psum_tensor(f"own{h}", [P, 512], f32)) for h in range(3)]

        src_in, dst_in, et_in = sem("src_in"), sem("dst_in"), sem("et_in")
        far_set, w_in, x_in = sem("far_set"), sem("w_in"), sem2("x_in")
        ident_zero, const_set, zeros_set = sem("ident_zero"), sem("const_set"), sem("zeros_set")
        src_cast, srcT_done, idx_done = sem("src_cast"), sem("srcT_done"), sem("idx_done")
        high_done, rest_done, middle_done = sem("high_done"), sem("rest_done"), sem("middle_done")
        low_done, again_done, parts_out = sem("low_done"), sem2("again_done"), sem("parts_out")
        et_cast = sem("et_cast")
        prep = sem("prep")
        krel_cast, krelT_done, krel_done = sem("krel_cast"), sem("krelT_done"), sem("krel_done")
        par_set, par_in, any_set = sem("par_set"), sem("par_in"), sem("any_set")
        xT_done, xT_taken = sem("xT_done"), sem("xT_taken")
        gidx_ready, rows_in, late_in = sem2("gidx_ready"), sem2("rows_in"), sem2("late_in")
        src_b_in, src_h_ready, pick_ready = sem2("src_b_in"), sem2("src_h_ready"), sem2("pick_ready")
        away_ready, act_pick_ready = sem("away_ready"), sem2("act_pick_ready")
        own_done, own_rows = sem2("own_done"), sem2("own_rows")
        onehot_ready, agg_ready, agg_copied = sem2("onehot_ready"), sem2("agg_ready"), sem2("agg_copied")
        rel_ready, rel_added = sem2("rel_ready"), sem("rel_added")
        out_zeroed, w_centered, x_centered = sem("out_zeroed"), sem("w_centered"), sem("x_centered")
        table_loaded = sem("table_loaded")
        y_done, sq_done, sqsum_done = sem("y_done"), sem("sq_done"), sem("sqsum_done")
        var_done, std_done, rstd_done = sem("var_done"), sem("std_done"), sem("rstd_done")
        y_ready, out_done = sem("y_ready"), sem("out_done")
        g_prep, g_setT, g_set, g_w_in = sem("g_prep"), sem("g_setT"), sem("g_set"), sem("g_w_in")
        g_idx_ready, g_rows_in = sem("g_idx_ready"), sem("g_rows_in")
        g_T_done, g_T_taken, g_all_done, g_msg_ready = sem("g_T_done"), sem("g_T_taken"), sem("g_all_done"), sem("g_msg_ready")
        g_step, g_added, g_sum = sem("g_step"), sem("g_added"), sem("g_sum")
        g_w_centered = sem("g_w_centered")
        g_sumT, g_final = sem("g_sumT"), sem("g_final")
        block = ctx.enter_context(nc.Block())

        def tile_view(t):
            return t[:, :].rearrange("g (j e) -> g j e", e=P)

        def group_loop(eng, body, first=0, last=LAST + 1):
            if first == 0:
                body(0)
                first = 1
            with eng.Fori(first, last) as i:
                body(i)

        def y_bank(n):
            bank = (own[0], own[1], own[2], rel)[n]
            k = YCUT[n + 1] - YCUT[n]
            return bank[0:NP, 0:k * D].rearrange("p (b d) -> p b d", d=D)

        def is_first(i):
            return isinstance(i, int) and i == 0

        def go_general(eng):
            eng.wait_ge(any_set, 1)
            v = nc.values_load_multi_w_load_instructions(any_far[0:1, 0:1], engines=[eng.engine], min_val=0, max_val=int(FAR),
                                                         skip_runtime_bounds_check_because="zero or FAR")[1][0]
            return eng.If(v > 0)

        @block.sync
        def _(sp):
            def load(tile, a, s, pad_src):
                sp.dma_start(tile[0:G - 1, :], a[0:(G - 1) * ROW].rearrange("(g e) -> g e", e=ROW)).then_inc(s, 16)
                sp.dma_start(tile[G - 1:G, 0:REAL], a[(G - 1) * ROW:E].rearrange("(o e) -> o e", o=1)).then_inc(s, 16)
                sp.dma_start(tile[G - 1:G, REAL:ROW], pad_src).then_inc(s, 16)

            def row(a):
                return a[E - PAD:E].rearrange("(o e) -> o e", o=1)

            load(src_i, src, src_in, row(src))
            load(dst_i, dst, dst_in, row(dst))
            sp.wait_ge(far_set, 1)
            load(et_i, etype, et_in, far_i[:, :])
            pv = x_parts.rearrange("(p b) d -> p b d", b=NB)
            for n in range(2):
                b0, b1 = XHALF[n], XHALF[n + 1]
                sp.wait_ge(high_done, n + 1)
                sp.wait_ge(middle_done, n + 1)
                sp.wait_ge(low_done, n + 1)
                sp.wait_ge(again_done[n], 1)
                sp.dma_start(pv[:, b0:b1, :], xp[:, b0:b1, :, :].rearrange("p b s d -> p b (s d)")).then_inc(parts_out, 16)

            def spread_sources(i, u):
                if not is_first(i):
                    sp.wait_ge(src_h_ready[u], i)
                a = src[bass.ds(i * (2 * ROW) + u * ROW, OWNW[u])]
                sp.dma_start(src_b[u][:, :], a.rearrange("(o e) -> o e", o=1).to_broadcast([NP, OWNW[u]])).then_inc(src_b_in[u], 16)

            def turn(i):
                spread_sources(i, 0)
                spread_sources(i, 1)
            turn(0)
            sp.wait_ge(par_set, 3)
            sp.dma_start(par_row[:, :], par[:, :]).then_inc(par_in, 16)
            group_loop(sp, turn, first=1)
            with go_general(sp):
                sp.dma_start(g_w[:, :, :], weight.rearrange("r k d -> k r d")).then_inc(g_w_in, 16)
            for n in range(YT):
                b0, b1 = YCUT[n], YCUT[n + 1]
                sp.wait_ge(y_ready, n + 1)
                sp.dma_start(out.rearrange("(p b) d -> p b d", b=NB)[:, b0:b1, :], y[:, b0:b1, :]).then_inc(out_done, 16)
            sp.wait_ge(out_done, 16 * YT)

        @block.gpsimd
        def _(pool):
            pool.memset(far_i[:, :], -int(FAR)).then_inc(far_set, 1)
            pool.memset(ident[:, :], 0.0).then_inc(ident_zero, 1)
            pool.iota(ramp[:, :, 0:R], pattern=[[R, WIN], [1, R]], base=0, channel_multiplier=0,
                      allow_small_or_imprecise_dtypes=True).then_inc(const_set, 1)
            pool.wait_ge(ident_zero, 1)
            pool.affine_select(out=ident[:, :], in_=ident[:, :], compare_op=ALU.not_equal, fill=1.0,
                               base=0, pattern=[[-1, P]], channel_multiplier=1).then_inc(const_set, 1)
            pool.iota(node[:, :], pattern=[[1, NB]], base=-MID, channel_multiplier=NB,
                      allow_small_or_imprecise_dtypes=True).then_inc(const_set, 1)
            pool.iota(node_neg[:, :], pattern=[[-1, NB]], base=MID, channel_multiplier=-NB,
                      allow_small_or_imprecise_dtypes=True).then_inc(const_set, 1)
            pool.memset(one[:, :], 1.0).then_inc(const_set, 1)
            pool.memset(zeros[:, :], 0.0).then_inc(zeros_set, 1)
            pool.memset(outT[:, :], 0.0).then_inc(out_zeroed, 1)
            pool.wait_ge(x_in[0], 16)
            pool.tensor_copy(xp[:, 0:XHALF[1], RP - 1, :], x_sb[:, 0:XHALF[1], :]).then_inc(again_done[0], 1)
            pool.wait_ge(parts_out, 32)

            def fetch(i, u):
                if not is_first(i):
                    pool.wait_ge(agg_ready[u], i)
                pool.wait_ge(gidx_ready[u], i + 1)
                pool.nop(nofuse=True)
                for j in range(OWN[u], GT):
                    pool.indirect_dma_start(
                        rows[:, u, j, :], None, x_parts,
                        bass.IndirectOffsetOnAxis(ap=gidx[:, u, j:j + 1], axis=0)).then_inc(rows_in[u] if j < LATE else late_in[u], 16)

            def turn(i):
                fetch(i, 0)
                fetch(i, 1)
            group_loop(pool, turn)

            with go_general(pool):
                pool.iota(g_ramp[:, :, :], pattern=[[1, NB], [NB, NP]], base=0, channel_multiplier=0,
                          allow_small_or_imprecise_dtypes=True).then_inc(g_set, 1)
                with pool.Fori(0, TILES) as t:
                    pool.wait_ge(g_idx_ready, t + 1)
                    pool.nop(nofuse=True)
                    pool.indirect_dma_start(g_rows[:, :], None, x,
                                            bass.IndirectOffsetOnAxis(ap=g_idx[:, 0:1], axis=0)).then_inc(g_rows_in, 16)

        @block.scalar
        def _(act):
            for n in range(2):
                b0, b1 = XHALF[n], XHALF[n + 1]
                act.dma_start(x_sb[:, b0:b1, :], x.rearrange("(p b) d -> p b d", b=NB)[:, b0:b1, :]).then_inc(x_in[n], 16)
            for q in range(2):
                act.dma_start(w_pair[q * D:(q + 1) * D, :, :],
                              weight.rearrange("(q two) k d -> two k q d", two=2)[q]).then_inc(w_in, 16)
            for n in range(2):
                b0, b1 = XHALF[n], XHALF[n + 1]
                act.wait_ge(x_in[n], 16)
                act.activation(xp[:, b0:b1, 0, :], x_sb[:, b0:b1, :], ACT.Copy).then_inc(high_done, 1)
            for n in range(2):
                b0, b1 = XHALF[n], XHALF[n + 1]
                act.wait_ge(rest_done, n + 1)
                act.activation(xp[:, b0:b1, 1, :], x_rest[:, b0:b1, :], ACT.Copy).then_inc(middle_done, 1)
            act.activation(xp[:, XHALF[1]:NB, RP - 1, :], x_sb[:, XHALF[1]:NB, :], ACT.Copy).then_inc(again_done[1], 1)
            act.wait_ge(src_in, 48)
            act.activation(src_f[:, :], src_i[:, :], ACT.Copy).then_inc(src_cast, 1)
            act.wait_ge(srcT_done, 1)
            iv = idx[:, :].rearrange("p (g j) -> p j g", j=GT)
            for n, (j0, j1) in enumerate(((0, 8), (8, GT))):
                act.activation(iv[:, j0:j1, :], own[n][:, 0:(j1 - j0) * G].rearrange("p (j g) -> p j g", g=G), ACT.Copy).then_inc(idx_done, 1)
            act.wait_ge(idx_done, 2)

            def group_indices(i, u):
                if not is_first(i):
                    act.wait_ge(late_in[u], i * (16 * (GT - LATE)))
                act.activation(gidx[:, u, :], idx[:, bass.ds(i * (2 * GT) + u * GT, GT)], ACT.Copy).then_inc(gidx_ready[u], 1)

            def narrow_sources(i, u):
                act.wait_ge(src_b_in[u], (i + 1) * 16)
                if not is_first(i):
                    act.wait_ge(pick_ready[u], i * VPICK)
                    act.wait_ge(act_pick_ready[u], i)
                act.activation(src_h[u][:, :, 0:CUTW[u]], src_b[u][:, :].rearrange("p (c w) -> p c w", c=CUT), ACT.Copy, bias=-float(MID)).then_inc(src_h_ready[u], 1)

            def clear_agg(u):
                act.activation(agg[u][:, :, :], zeros[:, :].rearrange("p (h k) -> p h k", h=2), ACT.Copy).then_inc(agg_copied[u], 1)

            def take_agg(i, u):
                act.wait_ge(agg_ready[u], i + 1)
                if not is_first(i):
                    act.wait_ge(rel_ready[u], i)
                for q in range(2):
                    act.activation(aggT[q * D:(q + 1) * D, u, :, :],
                                   agg[u][q * D:(q + 1) * D, :, :].rearrange("d h (n r two) -> d (h n) r two", r=RQ, two=2)[:, :, :, q],
                                   ACT.Copy).then_inc(agg_copied[u], 1)
                act.wait_ge(agg_copied[u], i * 3 + 3)
                clear_agg(u)

            def act_picks(i, u, part):
                if part == 0:
                    if not is_first(i):
                        act.wait_ge(own_done[u], i * OWN[u])
                        act.wait_ge(act_pick_ready[u], i)
                        act.wait_ge(act_pick_ready[1 - u], i + u)
                    elif u == 1:
                        act.wait_ge(act_pick_ready[0], 1)
                    act.wait_ge(src_h_ready[u], i + 1)
                cuts = (0, APICK // 2, APICK)
                b0, b1 = cuts[part % 2], cuts[part % 2 + 1]
                if part < 2:
                    for b in range(b0, b1):
                        last = act.activation(away[:, b, 0:OWNW[u]].rearrange("p (c w) -> p c w", c=CUT), src_h[u][:, :, 0:CUTW[u]], ACT.Abs,
                                              bias=node_neg[:, VPICK + b:VPICK + b + 1])
                    last.then_inc(away_ready, 1)
                else:
                    act.wait_ge(away_ready, i * 4 + (2 * u + part - 1))
                    for b in range(b0, b1):
                        last = act.activation(pick[u][:, VPICK + b, :], away[:, b, 0:OWNW[u]], ACT.Relu, bias=one[:, :], scale=-1.0)
                    if part == 3:
                        last.then_inc(act_pick_ready[u], 1)

            def take_own(i, u, between=lambda h: None):
                for h in range(OWN[u]):
                    act.wait_ge(own_done[u], i * OWN[u] + (h + 1))
                    act.activation(rows[:, u, h, 0:SPLIT * D], own[h % 3][:, 0:SPLIT * D], ACT.Copy).then_inc(own_rows[u], 1)
                    act.activation(rows[:, u, h, SPLIT * D:RP * D], own[h % 3][:, 0:D], ACT.Copy).then_inc(own_rows[u], 1)
                    between(h)

            group_indices(0, 0)
            group_indices(0, 1)
            act.wait_ge(et_in, 48)
            act.activation(et_f[:, :], et_i[:, :], ACT.Copy).then_inc(et_cast, 1)
            narrow_sources(0, 0)
            act.wait_ge(const_set, 5)
            for part in range(3):
                act_picks(0, 0, part)
            act.wait_ge(krelT_done, 1)
            kv = krel[:, :].rearrange("p (g j) -> p j g", j=GT)
            for n, (j0, j1) in enumerate(((0, 8), (8, GT))):
                act.activation(kv[:, j0:j1, :], agg[1][:, n, 0:(j1 - j0) * G].rearrange("p (j g) -> p j g", g=G), ACT.Copy).then_inc(krel_done, 1)
            act_picks(0, 0, 3)
            narrow_sources(0, 1)
            act.wait_ge(zeros_set, 1)
            clear_agg(0)
            act_picks(0, 1, 0)
            act_picks(0, 1, 1)
            take_own(0, 0)
            act_picks(0, 1, 2)
            act_picks(0, 1, 3)
            act.wait_ge(krel_done, 2)
            clear_agg(1)

            def turn(i, more=True):
                if more:
                    narrow_sources(i + 1, 0)
                    group_indices(i + 1, 0)
                take_agg(i, 0)
                take_own(i, 1, lambda h: act_picks(i + 1, 0, h) if more else None)
                if more:
                    act_picks(i + 1, 0, 3)
                if more:
                    narrow_sources(i + 1, 1)
                    group_indices(i + 1, 1)
                take_agg(i, 1)
                if more:
                    take_own(i + 1, 0, lambda h: act_picks(i + 1, 1, h))
                    act_picks(i + 1, 1, 3)
            group_loop(act, turn, last=LAST)
            turn(LAST, more=False)

            with go_general(act):
                with act.Fori(0, TILES) as t:
                    act.wait_ge(g_step, t + 1)
                    act.activation(g_idx[:, :], idx[:, bass.ds(t, 1)], ACT.Copy).then_inc(g_idx_ready, 1)
                    act.wait_ge(g_T_done, t + 1)
                    act.activation(g_rowsT[:, :], rel[0:D, 0:P], ACT.Copy).then_inc(g_T_taken, 1)
            act.activation(std[:, 0:1], one[:, :], ACT.Sqrt).then_inc(table_loaded, 1)
            act.wait_ge(table_loaded, 1)
            for n in range(YT + 1):
                if n < YT:
                    b0, b1 = YCUT[n], YCUT[n + 1]
                    act.wait_ge(y_done, n + 1)
                    act.activation(sq[:, b0:b1, :], y_bank(n), ACT.Square).then_inc(sq_done, 1)
                if n >= 1:
                    b0, b1 = YCUT[n - 1], YCUT[n]
                    act.wait_ge(var_done, n)
                    act.activation(std[:, b0:b1], var[:, b0:b1], ACT.Sqrt).then_inc(std_done, 1)

        @block.vector
        def _(dve):
            v = nc.vector
            def picks(i, u):
                dve.wait_ge(src_h_ready[u], i + 1)
                if not is_first(i):
                    dve.wait_ge(own_done[u], i * OWN[u])
                for b in range(VPICK):
                    v.tensor_scalar(pick[u][:, b, :], src_h[u][:, :, 0:CUTW[u]], node[:, b:b + 1], None, ALU.is_equal).then_inc(pick_ready[u], 1)

            steps = [0]

            def step(ins):
                steps[0] += 1
                ins.then_inc(prep, 1)

            def settle():
                dve.wait_ge(prep, steps[0])

            for n in range(2):
                b0, b1 = XHALF[n], XHALF[n + 1]
                dve.wait_ge(high_done, n + 1)
                v.tensor_tensor(x_rest[:, b0:b1, :], x_sb[:, b0:b1, :], xp[:, b0:b1, 0, :], ALU.subtract).then_inc(rest_done, 1)
            for n in range(2):
                b0, b1 = XHALF[n], XHALF[n + 1]
                dve.wait_ge(middle_done, n + 1)
                v.tensor_tensor(xp[:, b0:b1, 2, :], x_rest[:, b0:b1, :], xp[:, b0:b1, 1, :], ALU.subtract).then_inc(low_done, 1)
            dve.wait_ge(dst_in, 48)
            step(v.tensor_copy(dst_f[:, :], dst_i[:, :]))
            settle()
            step(v.tensor_reduce(tmin[:, :], tile_view(dst_f), AX.X, ALU.min))
            step(v.tensor_reduce(tmax[:, :], tile_view(dst_f), AX.X, ALU.max))
            settle()
            for h in range(2):
                step(v.tensor_reduce(base[:, h:h + 1], tmin[:, HALF[h]:HALF[h + 1]], AX.X, ALU.min))
            settle()
            for h in range(2):
                a, b = HALF[h], HALF[h + 1]
                step(v.tensor_scalar(start[:, a:b], tmin[:, a:b], base[:, h:h + 1], float(SPAN - WIN), ALU.subtract, ALU.min))
            settle()
            v.tensor_scalar(par[:, 0:GT], start[:, :], float(R), None, ALU.mult).then_inc(par_set, 1)
            v.tensor_copy(par[:, GT:GT + 2], base[:, :]).then_inc(par_set, 1)
            for h in range(2):
                a, b = HALF[h], HALF[h + 1]
                step(v.tensor_scalar(wstart[:, a:b], start[:, a:b], base[:, h:h + 1], None, ALU.add))
            settle()
            step(v.tensor_tensor(reach[:, :], tmax[:, :], wstart[:, :], ALU.subtract))
            settle()
            step(v.tensor_scalar(far[:, :], reach[:, :], float(WIN), FAR, ALU.is_ge, ALU.mult))
            settle()
            v.tensor_reduce(par[:, GT + 2:PW], far[:, :], AX.X, ALU.max).then_inc(par_set, 1)
            step(v.scalar_tensor_tensor(shift[:, :], wstart[:, :], float(R), far[:, :], ALU.mult, ALU.add))
            settle()
            dve.wait_ge(et_cast, 1)
            dve.wait_ge(srcT_done, 1)
            step(v.scalar_tensor_tensor(key_f[:, :], dst_f[:, :], float(R), et_f[:, :], ALU.mult, ALU.add))
            settle()
            v.tensor_tensor(tile_view(krel_f), tile_view(key_f),
                            shift[:, :].rearrange("g (j o) -> g j o", o=1).to_broadcast([G, GT, P]), ALU.subtract).then_inc(krel_cast, 1)
            dve.wait_ge(const_set, 5)
            picks(0, 0)
            dve.wait_ge(krel_done, 2)

            def onehots(i, u):
                if not is_first(i):
                    dve.wait_ge(agg_ready[u], i)
                for j in range(GT):
                    last = v.tensor_scalar(onehot[:, u, j, :], ramp[:, :, 0:R],
                                           krel[:, bass.ds(i * (2 * GT) + (u * GT + j), 1)], None, ALU.is_equal)
                last.then_inc(onehot_ready[u], 1)

            def half_starts(i, u):
                return nc.values_load_multi_w_load_instructions(
                    par_row[0:1, bass.ds(i * (2 * PW) + (u * PW + GT), 2)], engines=[DVE_ENG], min_val=0, max_val=N - 1,
                    skip_runtime_bounds_check_because="a node index of the edge list")[1]

            def add_rel(i, u, at):
                if is_first(i) and u == 0:
                    dve.wait_ge(out_zeroed, 1)
                dve.wait_ge(rel_ready[u], i + 1)
                for h in range(2):
                    if not (is_first(i) and u == 0 and h == 0):
                        dve.wait_ge(rel_added, i * 4 + (2 * u + h))
                    o = outT[:, bass.ds(at[h], SPAN)]
                    v.tensor_tensor(o, o, rel[0:D, h * SPAN:(h + 1) * SPAN], ALU.add).then_inc(rel_added, 1)

            onehots(0, 0)
            picks(0, 1)

            def take_mean(t, mean, done, n):
                v.tensor_reduce(mean[:, :], t[:, :, :], AX.X, ALU.add).then_inc(done, 1)
                dve.wait_ge(done, 1)
                v.scalar_tensor_tensor(t[:, :, :], mean[:, :].rearrange("p (b o) -> p b o", o=1).to_broadcast([t.shape[0], n, D]),
                                       -1.0 / D, t[:, :, :], ALU.mult, ALU.add).then_inc(done, 1)

            dve.wait_ge(w_in, 32)
            take_mean(w_pair, w_mean, w_centered, RQ)
            dve.wait_ge(par_in, 16)

            def add_x():
                ov = outT[:, 0:N].rearrange("d (p b) -> d b p", b=NB)
                dve.wait_ge(rel_added, 4 * LAST + 2)
                for n in range(XT):
                    b0, k = n * XB, min(XB, NB - n * XB)
                    dve.wait_ge(xT_done, n + 1)
                    o = ov[:, b0:b0 + k, :]
                    v.tensor_tensor(o, o, own[n % 3][0:D, 0:k * NP].rearrange("d (b p) -> d b p", p=NP), ALU.add).then_inc(xT_taken, 1)
                dve.wait_ge(xT_taken, XT)

            def turn(i, more=True):
                at = [half_starts(i, u) for u in range(2)]
                if not more:
                    dve.wait_ge(again_done[0], 1)
                    dve.wait_ge(again_done[1], 1)
                    take_mean(x_sb, x_mean, x_centered, NB)
                onehots(i, 1)
                if more:
                    picks(i + 1, 0)
                add_rel(i, 0, at[0])
                if not more:
                    add_x()
                if more:
                    onehots(i + 1, 0)
                    picks(i + 1, 1)
                add_rel(i, 1, at[1])
            group_loop(dve, turn, last=LAST)
            v.tensor_reduce(any_far[:, :], par_row[:, :].rearrange("o (g w) -> o g w", w=PW)[:, :, PW - 1:PW].rearrange("o g w -> o (g w)"),
                            AX.X, ALU.max).then_inc(any_set, 1)
            turn(LAST, more=False)

            def finish(n):
                b0, b1 = YCUT[n], YCUT[n + 1]
                dve.wait_ge(std_done, n + 1)
                v.reciprocal(rstd[:, b0:b1], std[:, b0:b1]).then_inc(rstd_done, 1)
                dve.wait_ge(rstd_done, n + 1)
                v.tensor_tensor(y[:, b0:b1, :], y_bank(n),
                                rstd[:, b0:b1].rearrange("p (b o) -> p b o", o=1).to_broadcast([NP, b1 - b0, D]),
                                ALU.mult).then_inc(y_ready, 1)

            with go_general(dve):
                dve.wait_ge(g_w_in, 16)
                g_mean = sqsum[0:D, 0:R]
                v.tensor_reduce(g_mean, g_w[:, :, :], AX.X, ALU.add).then_inc(g_w_centered, 1)
                dve.wait_ge(g_w_centered, 1)
                v.scalar_tensor_tensor(g_w[:, :, :], g_mean.rearrange("p (b o) -> p b o", o=1).to_broadcast([D, R, D]),
                                       -1.0 / D, g_w[:, :, :], ALU.mult, ALU.add).then_inc(g_w_centered, 1)
                v.tensor_scalar(shift[:, :], far[:, :], -FAR, None, ALU.add).then_inc(g_prep, 1)
                dve.wait_ge(g_prep, 1)
                v.tensor_tensor(tile_view(g_dst_f), tile_view(dst_f),
                                shift[:, :].rearrange("g (j o) -> g j o", o=1).to_broadcast([G, GT, P]), ALU.add).then_inc(g_prep, 1)
                for n, a in enumerate((g_dst, g_et)):
                    av = a[:, :].rearrange("p (g j) -> p j g", j=GT)
                    dve.wait_ge(g_setT, n + 1)
                    for m, (j0, j1) in enumerate(((0, 8), (8, GT))):
                        v.tensor_copy(av[:, j0:j1, :], own[m][:, 0:(j1 - j0) * G].rearrange("p (j g) -> p j g", g=G)).then_inc(g_set, 1)
                dve.wait_ge(own_done[1], (LAST + 1) * OWN[1])
                dve.wait_ge(g_set, 5)
                v.memset(g_msg[:, :], 0.0).then_inc(g_step, 1)
                with dve.Fori(0, TILES) as t:
                    dve.wait_ge(g_step, t + 1)
                    v.tensor_scalar(g_rel[:, :], ramp[:, 0, 0:R], g_et[:, bass.ds(t, 1)], None, ALU.is_equal).then_inc(g_msg_ready, 1)
                    v.tensor_scalar(g_hot[:, :, :], g_ramp[:, :, :], g_dst[:, bass.ds(t, 1)], None, ALU.is_equal).then_inc(g_msg_ready, 1)
                    dve.wait_ge(g_msg_ready, t * 5 + 1)
                    dve.wait_ge(g_all_done, t + 1)
                    for m in range(2):
                        r0 = m * (R // 2)
                        v.tensor_tensor(g_all[:, r0:r0 + R // 2, :], own[m][:, :].rearrange("p (r d) -> p r d", d=D),
                                        g_rel[:, r0:r0 + R // 2].rearrange("p (r o) -> p r o", o=1).to_broadcast([P, R // 2, D]),
                                        ALU.mult).then_inc(g_msg_ready, 1)
                    dve.wait_ge(g_msg_ready, t * 5 + 4)
                    v.tensor_reduce(g_msg[:, :], g_all[:, :, :].rearrange("p r d -> p d r"), AX.X, ALU.add).then_inc(g_msg_ready, 1)
                dve.wait_ge(g_added, 1)
                yv = y[:, :, :].rearrange("p b d -> p (b d)")
                for n in range(-(-NB // YB)):
                    c0, c1 = n * YB * D, min((n + 1) * YB, NB) * D
                    v.tensor_copy(yv[:, c0:c1], agg[n // 2][0:NP, n % 2, 0:c1 - c0]).then_inc(g_sum, 1)
                ov = outT[:, 0:N].rearrange("d (p b) -> d b p", b=NB)
                dve.wait_ge(rel_added, 2 * G)
                for n in range(XT):
                    b0, k = n * XB, min(XB, NB - n * XB)
                    dve.wait_ge(g_sumT, n + 1)
                    o = ov[:, b0:b0 + k, :]
                    v.tensor_tensor(o, o, own[n % 3][0:D, 0:k * NP].rearrange("d (b p) -> d b p", p=NP), ALU.add).then_inc(g_final, 1)

            for n in range(YT):
                b0, b1 = YCUT[n], YCUT[n + 1]
                dve.wait_ge(sq_done, n + 1)
                v.tensor_reduce(sqsum[:, b0:b1], sq[:, b0:b1, :], AX.X, ALU.add).then_inc(sqsum_done, 1)
                dve.wait_ge(sqsum_done, n + 1)
                v.tensor_scalar(var[:, b0:b1], sqsum[:, b0:b1], 1.0 / D, EPS, ALU.mult, ALU.add).then_inc(var_done, 1)
                if n >= 1:
                    finish(n - 1)
            finish(YT - 1)

        @block.tensor
        def _(pe):
            def edge_transposes(a, banks, done):
                for j in range(GT):
                    last = nc.tensor.transpose(banks[j // 8][:, (j % 8) * G:(j % 8 + 1) * G],
                                               a[:, j * P:(j + 1) * P], ident[0:G, 0:G])
                last.then_inc(done, 1)

            pe.wait_ge(const_set, 5)
            pe.wait_ge(src_cast, 1)
            edge_transposes(src_f, own[0:2], srcT_done)

            def fetch_own(i, u):
                if not is_first(i):
                    pe.wait_ge(pick_ready[u], (i + 1) * VPICK)
                    pe.wait_ge(act_pick_ready[u], i + 1)
                if u == 1:
                    pe.wait_ge(own_rows[0], (i + 1) * (2 * OWN[0]))
                elif not is_first(i):
                    pe.wait_ge(own_rows[1], i * (2 * OWN[1]))
                def product(h, b):
                    return nc.tensor.matmul(own[h][:, 0:SPLIT * D], pick[u][:, b, h * P:(h + 1) * P],
                                            xp[:, b, 0:SPLIT, :].rearrange("p s d -> p (s d)"), start=(b == 0), stop=(b == NB - 1))
                if is_first(i):
                    for b in range(NB):
                        if b < VPICK:
                            pe.wait_ge(pick_ready[u], b + 1)
                        elif b == VPICK:
                            pe.wait_ge(act_pick_ready[u], 1)
                        for h in range(OWN[u]):
                            last = product(h, b)
                            if b == NB - 1:
                                last.then_inc(own_done[u], 1)
                else:
                    for h in range(OWN[u]):
                        for b in range(NB):
                            last = product(h, b)
                        last.then_inc(own_done[u], 1)

            def window_starts(i, u):
                return nc.values_load_multi_w_load_instructions(
                    par_row[0:1, bass.ds(i * (2 * PW) + u * PW, GT)], engines=[PE_ENG], min_val=0, max_val=(SPAN - WIN) * R,
                    skip_runtime_bounds_check_because="clamped when it was worked out")[1]

            def aggregate(i, u, at):
                pe.wait_ge(agg_copied[u], i * 3 + 1)
                pe.wait_ge(onehot_ready[u], i + 1)
                pe.wait_ge(own_rows[u], (i + 1) * (2 * OWN[u]))
                for j in range(GT):
                    if j == OWN[u]:
                        pe.wait_ge(rows_in[u], (i + 1) * (16 * (LATE - OWN[u])))
                    if j == LATE:
                        pe.wait_ge(late_in[u], (i + 1) * (16 * (GT - LATE)))
                    for s in range(SPLIT):
                        last = nc.tensor.matmul(
                            agg[u][:, int(j >= HALF[1]), bass.ds(at[j], KEYS)],
                            rows[:, u, j, s * D:(s + 2) * D], onehot[:, u, j, :],
                            start=(j in HALF and s == 0), stop=(j + 1 in HALF and s == SPLIT - 1), skip_group_check=True)
                last.then_inc(agg_ready[u], 1)

            def relate(i, u):
                pe.wait_ge(agg_copied[u], i * 3 + 3)
                if not (is_first(i) and u == 0):
                    pe.wait_ge(rel_added, i * 4 + 2 * u)
                for q in range(RQ):
                    last = nc.tensor.matmul(rel[0:D, 0:2 * SPAN], w_pair[:, q, :], aggT[:, u, :, q],
                                            start=(q == 0), stop=(q == RQ - 1))
                last.then_inc(rel_ready[u], 1)

            pe.wait_ge(idx_done, 2)
            pe.wait_ge(krel_cast, 1)
            edge_transposes(krel_f, (agg[1][:, 0, :], agg[1][:, 1, :]), krelT_done)
            fetch_own(0, 0)
            pe.wait_ge(par_in, 16)

            aggregate(0, 0, window_starts(0, 0))

            def transpose_x(n0, n1):
                pe.wait_ge(x_centered, 2)
                pe.wait_ge(own_rows[1], (LAST + 1) * (2 * OWN[1]))
                for n in range(n0, n1):
                    if n >= 3:
                        pe.wait_ge(xT_taken, n - 2)
                    for b in range(n * XB, min((n + 1) * XB, NB)):
                        c = (b - n * XB) * NP
                        last = nc.tensor.transpose(own[n % 3][0:D, c:c + NP], x_sb[:, b, :], ident[0:NP, 0:NP])
                    last.then_inc(xT_done, 1)

            def turn(i, more=True):
                at = window_starts(i, 1)
                fetch_own(i, 1)
                if is_first(i):
                    pe.wait_ge(w_centered, 2)
                relate(i, 0)
                if not more:
                    transpose_x(0, 3)
                aggregate(i, 1, at)
                if not more:
                    transpose_x(3, XT)
                if more:
                    at = window_starts(i + 1, 0)
                    fetch_own(i + 1, 0)
                relate(i, 1)
                if more:
                    aggregate(i + 1, 0, at)
            group_loop(pe, turn, last=LAST)
            turn(LAST, more=False)

            with go_general(pe):
                pe.wait_ge(g_prep, 2)
                pe.wait_ge(xT_taken, XT)
                pe.wait_ge(agg_copied[0], (LAST + 1) * 3 + 1)
                pe.wait_ge(agg_copied[1], (LAST + 1) * 3 + 1)
                edge_transposes(g_dst_f, own[0:2], g_setT)
                pe.wait_ge(g_set, 3)
                edge_transposes(et_f, own[0:2], g_setT)
                for n in range(4):
                    nc.tensor.matmul(agg[n // 2][:, n % 2, :], zeros[:, 0:P], zeros[:, 0:512], start=True, stop=False, skip_group_check=True)
                pe.wait_ge(g_set, 5)
                pe.wait_ge(g_w_centered, 2)
                with pe.Fori(0, TILES) as t:
                    pe.wait_ge(g_rows_in, (t + 1) * 16)
                    pe.nop(nofuse=True)
                    nc.tensor.transpose(rel[0:D, 0:P], g_rows[:, :], ident[:, :]).then_inc(g_T_done, 1)
                    pe.wait_ge(g_T_taken, t + 1)
                    pe.nop(nofuse=True)
                    for m in range(2):
                        last = nc.tensor.matmul(own[m][:, :], g_rowsT[:, :], g_w[:, m * (R // 2):(m + 1) * (R // 2), :], start=True, stop=True)
                    last.then_inc(g_all_done, 1)
                    pe.wait_ge(g_msg_ready, (t + 1) * 5)
                    for b in range(NB):
                        n, c = b // YB, (b % YB) * D
                        last = nc.tensor.matmul(agg[n // 2][0:NP, n % 2, c:c + D], g_hot[:, b, :], g_msg[:, :],
                                                start=False, stop=False, skip_group_check=True)
                    last.then_inc(g_step, 1)
                nc.tensor.matmul(rel[0:D, 0:D], zeros[:, 0:D], zeros[:, 0:D], start=True, stop=True).then_inc(g_added, 1)
                for n in range(XT):
                    pe.wait_ge(g_sum, -(-min((n + 1) * XB, NB) // YB))
                    if n >= 3:
                        pe.wait_ge(g_final, n - 2)
                    for b in range(n * XB, min((n + 1) * XB, NB)):
                        c = (b - n * XB) * NP
                        last = nc.tensor.transpose(own[n % 3][0:D, c:c + NP], y[:, b, :], ident[0:NP, 0:NP])
                    last.then_inc(g_sumT, 1)
                pe.wait_ge(g_final, XT)

            pe.wait_ge(rel_added, 2 * G)
            pe.wait_ge(xT_taken, XT)
            yv = outT[:, 0:N].rearrange("d (p b) -> d b p", b=NB)
            for n in range(YT):
                for b in range(YCUT[n], YCUT[n + 1]):
                    last = nc.tensor.transpose(y_bank(n)[:, b - YCUT[n], :], yv[:, b, :], ident[0:D, 0:D])
                last.then_inc(y_done, 1)


def kernel(x, src, dst, edge_type_16, L0_gnn_weight):
    import numpy as np
    import concourse.bacc as bacc
    from concourse import mybir as mb
    from concourse.bass_utils import run_bass_kernel_spmd

    nc = bacc.Bacc("TRN2", target_bir_lowering=False, num_devices=1)
    arrays = {"x": x, "src": src, "dst": dst, "edge_type": edge_type_16, "weight": L0_gnn_weight}
    arrays = {f"in_{k}": np.ascontiguousarray(v) for k, v in arrays.items()}
    args = [nc.dram_tensor(k, v.shape, mb.dt.from_np(v.dtype), kind="ExternalInput").ap() for k, v in arrays.items()]
    out = nc.dram_tensor("out", arrays["in_x"].shape, mb.dt.float32, kind="ExternalOutput").ap()
    gnn_resnorm(nc, *args, out)
    return run_bass_kernel_spmd(nc, [arrays], core_ids=[0]).results[0]["out"]
```
